# Optimizing a Trainium2 kernel written in Bass

```python
import numpy as np
import jax
import jax.numpy as jnp

def _softmax(x, axis=-1):
    return jax.nn.softmax(x, axis=axis)

def _gelu(x):
    return jax.nn.gelu(x, approximate=True)

def _silu(x):
    return jax.nn.silu(x)

def _sigmoid(x):
    return jax.nn.sigmoid(x)

def _layernorm(x, axis=-1, eps=1e-05):
    m = jnp.mean(x, axis=axis, keepdims=True)
    v = jnp.var(x, axis=axis, keepdims=True)
    return (x - m) / jnp.sqrt(v + eps)

def _scatter_add(tgt, idx, src, axis=0):
    return tgt.at[idx].add(src)

def _segment_sum(src, seg, n):
    return jax.ops.segment_sum(src, seg, n)
kernel_name = 'mk_conv_preact_d2_conv_nchw256_r2_5adcac'

def setup_inputs(seed: int=0):
    np.random.seed(seed)
    _w = jnp.asarray

    def _rec_inputs():
        import jax
        import jax.numpy as jnp
        _gk = jax.random.key(seed)
        x = -0.0003929 + 0.9999 * jax.random.normal(jax.random.fold_in(_gk, 1), (16, 128, 32, 32), jnp.float32)
        return x
    x = _rec_inputs()

    def _L0_conv_setup():
        import jax, jax.numpy as jnp
        import numpy as np
        from jax import lax
        BN_EPS = 1e-05
        key = jax.random.key(seed)
        ks = jax.random.split(key, 4)
        B, C1, H, W = (16, 128, 32, 32)
        E, C2, K = (4, 128, 3)
        x = jax.random.normal(ks[0], (B, C1, H, W), dtype=jnp.float32)
        w_route = jax.random.normal(ks[1], (E, C1), dtype=jnp.float32) * 0.02
        b_route = jnp.zeros((E,), dtype=jnp.float32)
        w_experts = jax.random.normal(ks[2], (E, C2, C1, K, K), dtype=jnp.float32) * 0.02
        bn_gamma = jnp.ones((C2,), dtype=jnp.float32)
        bn_beta = jnp.zeros((C2,), dtype=jnp.float32)
        bn_mean = jnp.zeros((C2,), dtype=jnp.float32)
        bn_var = jnp.ones((C2,), dtype=jnp.float32)
        return {'x': x, 'w_route': w_route, 'b_route': b_route, 'w_experts': w_experts, 'bn_gamma': bn_gamma, 'bn_beta': bn_beta, 'bn_mean': bn_mean, 'bn_var': bn_var}
    _L0_conv_all = _L0_conv_setup()
    _L0_conv_in = {k: v for k, v in _L0_conv_all.items() if k in ('w_route', 'b_route', 'w_experts', 'bn_gamma', 'bn_beta', 'bn_mean', 'bn_var')}
    del _L0_conv_all

    def _L1_conv_setup():
        import jax, jax.numpy as jnp
        import numpy as np
        key = jax.random.key(seed)
        kx, kw = jax.random.split(key)
        x = jax.random.normal(kx, (32, 128, 56, 56), dtype=jnp.float32)
        W = jax.random.normal(kw, (128, 128, 3, 3), dtype=jnp.float32)
        return {'x': x, 'W': W}
    _L1_conv_all = _L1_conv_setup()
    _L1_conv_in = {k: v for k, v in _L1_conv_all.items() if k in ('W',)}
    del _L1_conv_all
    return {'x': x, 'L0_conv_w_route': _L0_conv_in['w_route'], 'L0_conv_b_route': _L0_conv_in['b_route'], 'L0_conv_w_experts': _L0_conv_in['w_experts'], 'L0_conv_bn_gamma': _L0_conv_in['bn_gamma'], 'L0_conv_bn_beta': _L0_conv_in['bn_beta'], 'L0_conv_bn_mean': _L0_conv_in['bn_mean'], 'L0_conv_bn_var': _L0_conv_in['bn_var'], 'L1_conv_W': _L1_conv_in['W']}

def reference(x, L0_conv_w_route, L0_conv_b_route, L0_conv_w_experts, L0_conv_bn_gamma, L0_conv_bn_beta, L0_conv_bn_mean, L0_conv_bn_var, L1_conv_W):
    import jax
    import jax.numpy as jnp

    def _L0_conv_ref(x, w_route, b_route, w_experts, bn_gamma, bn_beta, bn_mean, bn_var):
        import jax, jax.numpy as jnp
        import numpy as np
        from jax import lax
        BN_EPS = 1e-05
        pooled = jnp.mean(x, axis=(2, 3))
        routing = jax.nn.sigmoid(pooled @ w_route.T + b_route)
        E, Co, Ci, kh, kw = w_experts.shape
        w = w_experts.reshape(E * Co, Ci, kh, kw)
        pad = kh // 2
        y = lax.conv_general_dilated(x, w, window_strides=(1, 1), padding=[(pad, pad), (pad, pad)], dimension_numbers=('NCHW', 'OIHW', 'NCHW'))
        B, _, Ho, Wo = y.shape
        y = y.reshape(B, E, Co, Ho, Wo)
        out = jnp.einsum('beohw,be->bohw', y, routing)
        inv = bn_gamma / jnp.sqrt(bn_var + BN_EPS)
        out = out * inv[None, :, None, None] + (bn_beta - bn_mean * inv)[None, :, None, None]
        return jax.nn.silu(out)

    def _L1_conv_ref(x, W):
        import jax, jax.numpy as jnp
        import numpy as np
        Wb = jnp.sign(W)
        out = jax.lax.conv_general_dilated(x, Wb, window_strides=(1, 1), padding=((1, 1), (1, 1)), rhs_dilation=(1, 1), dimension_numbers=('NCHW', 'OIHW', 'NCHW'), feature_group_count=1)
        return out

    def _gn(v, G=32, eps=1e-05):
        B_, C_, H_, W_ = v.shape
        g = v.reshape(B_, G, C_ // G, H_, W_)
        m = jnp.mean(g, axis=(2, 3, 4), keepdims=True)
        s = jnp.var(g, axis=(2, 3, 4), keepdims=True)
        return ((g - m) / jnp.sqrt(s + eps)).reshape(v.shape)

    def _ln_c(v, eps=1e-06):
        m = jnp.mean(v, axis=1, keepdims=True)
        s = jnp.var(v, axis=1, keepdims=True)
        return (v - m) / jnp.sqrt(s + eps)

    def _ln_t(v, eps=1e-05):
        m = jnp.mean(v, axis=-1, keepdims=True)
        s = jnp.var(v, axis=-1, keepdims=True)
        return (v - m) / jnp.sqrt(s + eps)

    def _to_tokens(v):
        B_, C_, H_, W_ = v.shape
        return v.reshape(B_, C_, H_ * W_).transpose(0, 2, 1)

    def _from_tokens(t, like):
        B_, C_, H_, W_ = like.shape
        return t.transpose(0, 2, 1).reshape(B_, C_, H_, W_)
    x = x + _L0_conv_ref(_gn(x), L0_conv_w_route, L0_conv_b_route, L0_conv_w_experts, L0_conv_bn_gamma, L0_conv_bn_beta, L0_conv_bn_mean, L0_conv_bn_var)
    x = x + _L1_conv_ref(_gn(x), L1_conv_W)
    return x

_drawn_inputs = setup_inputs


def setup_inputs(seed=0):
    import zlib

    import numpy as np

    out = dict(_drawn_inputs(seed))
    spreads = {'L0_conv_b_route': (0.0, 0.381),
     'L0_conv_bn_gamma': (1.0, 0.2),
     'L0_conv_bn_beta': (0.0, 0.1),
     'L0_conv_bn_mean': (0.0, 0.1),
     'L0_conv_bn_var': (1.0, 0.2)}
    factors = {'L0_conv_w_route': 52.774}
    for name, (base, spread) in spreads.items():
        noise = np.random.default_rng([zlib.crc32(name.encode()), seed]).standard_normal(out[name].shape)
        drawn = base * np.exp(spread * noise) if base else spread * noise
        out[name] = jnp.asarray(drawn.astype(out[name].dtype))
    for name, factor in factors.items():
        out[name] = (out[name] * factor).astype(out[name].dtype)
    return out
```

```python
from contextlib import ExitStack

import numpy as np

import concourse.bass as bass
from concourse import mybir

F32 = mybir.dt.float32
F16 = mybir.dt.float16
ALU = mybir.AluOpType
ACT = mybir.ActivationFunctionType

B, C, H, W = 16, 128, 32, 32
E, K = 4, 3
HW = H * W
GROUPS = 32
GSIZE = C // GROUPS
PH, PW = H + 2, W + 2
TILES = H // 2
NU = 4
KCO = K * C
BANK = 512
GN_EPS = 1e-5
BN_EPS = 1e-5
ACT_SCALE = 256.0
MORDER = (1, 2, 0, 3)

P_GAMMA, P_BETA, P_MEAN, P_VAR, P_WROUTE, P_BROUTE, P_COLS = 0, 1, 2, 3, 4, 8, 12


def build(nc, x, w_experts, w_sign, params, group_avg, out):
    x_v = x.rearrange("b c h w -> b c (h w)")
    out_v = out.rearrange("b c h w -> b c (h w)")
    we_v = w_experts.rearrange("p k e x o -> p k e (x o)")
    ws_v = w_sign.rearrange("p y x o -> p (y x o)")

    with ExitStack() as ctx:
        def sb(name, shape, dt=F32):
            return ctx.enter_context(nc.sbuf_tensor(name, shape, dt))

        def psum(name, shape):
            return ctx.enter_context(nc.psum_tensor(name, shape, F32))

        def sem(name):
            return ctx.enter_context(nc.semaphore(name))

        X = sb("X", [C, B * HW])
        UE = sb("UE", [C, E, NU, KCO])
        g1 = sb("g1", [C, E, KCO])
        gsum = sb("gsum", [C, E, KCO])
        U = [sb(f"U{p}", [C, NU, KCO]) for p in range(2)]
        xn = sb("xn", [C, PH, PW])
        V = [sb(f"V{p}", [C, NU, TILES, PW]) for p in range(2)]
        m1s = sb("m1s", [C, BANK])
        m12 = sb("m12", [C, 2, BANK])
        y = sb("y", [C, H, W])
        hn = sb("hn", [C, HW])
        hi = sb("hi", [C, PH, PW], F16)
        lo = sb("lo", [C, PH, PW], F16)
        ws_raw = sb("ws_raw", [C, K * KCO])
        ws_neg = sb("ws_neg", [C, K * KCO], F16)
        ws = sb("ws", [C, K * KCO], F16)
        prm = sb("prm", [C, P_COLS])
        gavg = sb("gavg", [C, C])
        ones = sb("ones", [C, C])
        nhalf = sb("nhalf", [C, 1])
        bn_ve = sb("bn_ve", [C, 1])
        bn_rs = sb("bn_rs", [C, 1])
        bn_scale = sb("bn_scale", [C, 1])
        bn_mscale = sb("bn_mscale", [C, 1])
        bn_shift = sb("bn_shift", [C, 1])

        def chain(tag):
            return dict(parts=sb(f"parts_{tag}", [C, 2, 6]), mv=sb(f"mv_{tag}", [C, 2]),
                        dev=sb(f"dev_{tag}", [C, 1]), spread=sb(f"spread_{tag}", [C, 1]),
                        ve=sb(f"ve_{tag}", [C, 1]), rstd=sb(f"rstd_{tag}", [C, 1]),
                        bias=sb(f"bias_{tag}", [C, 1]))

        gin, gmid = chain("in"), chain("mid")
        pooled = sb("pooled", [C, E])
        logits = sb("logits", [C, E])
        th = sb("th", [C, E])
        route = sb("route", [C, E])

        pm = [psum(f"pm{k}", [C, BANK]) for k in range(NU)]
        pc = psum("pc", [C, 2, BANK])
        ps_in = psum("ps_in", [C, BANK])
        ps_mid = psum("ps_mid", [C, BANK])
        MEAN, VAR, LOG = slice(0, 1), slice(1, 2), slice(2, 2 + E)

        x_loaded = [sem("x_loaded0"), sem("x_loaded1")]
        we_loaded = [sem(f"we_loaded{e}") for e in range(E)]
        ws_loaded = sem("ws_loaded")
        prm_loaded = sem("prm_loaded")
        stored = sem("stored")
        zeroed = sem("zeroed")
        bn_ve_ready = sem("bn_ve_ready")
        bn_rs_ready = sem("bn_rs_ready")
        bn_ready = sem("bn_ready")
        ue_ready = sem("ue_ready")
        ws_ready = sem("ws_ready")

        def chain_sems(tag):
            return dict(mv=sem(f"mv_{tag}_ready"),
                        gmean=sem(f"gmean_{tag}_ready"), dev=sem(f"dev_{tag}_ready"),
                        spread=sem(f"spread_{tag}_ready"), gvar=sem(f"gvar_{tag}_ready"),
                        ve=sem(f"ve_{tag}_ready"), rstd=sem(f"rstd_{tag}_ready"),
                        bias=sem(f"bias_{tag}_ready"))

        s_in, s_mid = chain_sems("in"), chain_sems("mid")
        pooled_ready = sem("pooled_ready")
        plogits_ready = sem("plogits_ready")
        logits_ready = sem("logits_ready")
        tanh_ready = sem("tanh_ready")
        route_ready = sem("route_ready")
        xn_ready = sem("xn_ready")
        v_ready = sem("v_ready")
        mix_first = sem("mix_first")
        mixed = sem("mixed")
        m_ready = sem("m_ready")
        m1_copied = sem("m1_copied")
        m12_ready = sem("m12_ready")
        y_ready = sem("y_ready")
        silu_ready = sem("silu_ready")
        h_ready = sem("h_ready")
        hn_ready = sem("hn_ready")
        hi_ready = sem("hi_ready")
        lo_ready = sem("lo_ready")
        conv_ready = sem("conv_ready")
        out_ready = sem("out_ready")

        def img(i):
            return X[:, bass.ts(i, HW)]

        def has(i):
            return not isinstance(i, int) or 0 <= i < B

        def wait(eng, s, n):
            if not isinstance(n, int) or n > 0:
                eng.wait_ge(s, n)

        def apart(eng):
            eng.wait_ge(prm_loaded, 32)

        def pipeline(eng, step):
            lo_t, hi_t = 2, B - 2
            for t in range(-2, lo_t):
                step(t, t % 2)
            with eng.Fori(lo_t, hi_t - 1, 2) as t:
                step(t, 0)
                step(t + 1, 1)
            for t in range(hi_t, B + 2):
                step(t, t % 2)

        block = ctx.enter_context(nc.Block())

        @block.sync
        def _(sp):
            def load(i, p):
                sp.dma_start(img(i), x_v[i, :, :]).then_inc(x_loaded[p], 16)

            load(0, 0)
            sp.dma_start(prm[:], params).then_inc(prm_loaded, 16)
            sp.dma_start(gavg[:], group_avg).then_inc(prm_loaded, 16)
            for e in range(E):
                sp.dma_start(UE[:, e, 0, :], we_v[:, 0, e, :]).then_inc(we_loaded[e], 16)
                sp.dma_start(UE[:, e, NU - 1, :], we_v[:, 2, e, :]).then_inc(we_loaded[e], 16)
                sp.dma_start(g1[:, e, :], we_v[:, 1, e, :]).then_inc(we_loaded[e], 16)
            load(1, 1)
            sp.dma_start(ws_raw[:], ws_v).then_inc(ws_loaded, 16)
            with sp.Fori(2, B - 1, 2) as i:
                for p in range(2):
                    sp.wait_ge(x_loaded[p], i * 8)
                    load(i + p, p)
            with sp.Fori(0, B) as i:
                sp.wait_ge(out_ready, i + 1)
                sp.dma_start(out_v[i, :, :], img(i)).then_inc(stored, 16)
            sp.wait_ge(stored, 16 * B)

        @block.gpsimd
        def _(pool):
            nc.gpsimd.memset(nhalf[:], -0.5).then_inc(zeroed, 1)
            nc.gpsimd.memset(ones[:], 1.0).then_inc(zeroed, 1)
            nc.gpsimd.memset(xn[:], 0.0).then_inc(zeroed, 1)
            for p in range(2):
                nc.gpsimd.memset(V[p][:], 0.0).then_inc(zeroed, 1)
            nc.gpsimd.memset(hi[:], 0.0).then_inc(zeroed, 1)
            nc.gpsimd.memset(lo[:], 0.0).then_inc(zeroed, 1)
            pool.wait_ge(zeroed, 1)
            pool.wait_ge(bn_ve_ready, 1)
            nc.gpsimd.tensor_tensor(bn_rs[:], bn_ve[:], nhalf[:], ALU.pow).then_inc(bn_rs_ready, 1)

            def power(g, s, i):
                if has(i):
                    pool.wait_ge(s["ve"], i + 1)
                    nc.gpsimd.tensor_tensor(g["rstd"][:], g["ve"][:], nhalf[:], ALU.pow).then_inc(s["rstd"], 1)

            def step(t, p):
                power(gmid, s_mid, t - 1)
                power(gin, s_in, t + 2)

            pipeline(pool, step)

        @block.tensor
        def _(pe):
            def group_mean(g, s, ps, i):
                if has(i):
                    pe.wait_ge(s["mv"], i + 1)
                    nc.tensor.matmul(ps[:, MEAN], gavg[:], g["mv"][:, 0:1], start=True, stop=True) \
                      .then_inc(s["gmean"], 1)

            def group_var(g, s, ps, i):
                if has(i):
                    pe.wait_ge(s["spread"], i + 1)
                    nc.tensor.matmul(ps[:, VAR], gavg[:], g["spread"][:], start=True, stop=True) \
                      .then_inc(s["gvar"], 1)

            def route_logits(i):
                if has(i):
                    pe.wait_ge(pooled_ready, i + 1)
                    nc.tensor.matmul(ps_in[:, LOG], ones[:], pooled[:], start=True, stop=True) \
                      .then_inc(plogits_ready, 1)

            def condconv_row(t, p, n):
                if not has(t):
                    return
                k = MORDER[n]
                if n == 0:
                    pe.wait_ge(v_ready, t + 1)
                    pe.wait_ge(mixed, (E - 1) * (t + 1))
                if k == 1:
                    wait(pe, m1_copied, t)
                elif k == 2:
                    wait(pe, m12_ready, 2 * t)
                else:
                    wait(pe, y_ready, 2 * t - (1 if k == 0 else 0))
                for kx in range(K):
                    mm = nc.tensor.matmul(pm[k][:], U[p][:, k, kx * C:(kx + 1) * C],
                                          V[p][:, k, :, kx:kx + W], start=(kx == 0), stop=(kx == K - 1))
                mm.then_inc(m_ready, 1)

            def sign_tap(i, tap):
                ky, kx = tap // K, tap % K
                if tap == 0:
                    pe.wait_ge(hi_ready, i + 1)
                    pe.wait_ge(lo_ready, i + 1)
                    wait(pe, out_ready, i)
                for part in (hi, lo):
                    for half in range(2):
                        r = half * (H // 2) + ky
                        mm = nc.tensor.matmul(pc[:, half, :], ws[:, tap * C:(tap + 1) * C],
                                              part[:, r:r + H // 2, kx:kx + W],
                                              start=(tap == 0 and part is hi),
                                              stop=(tap == K * K - 1 and part is lo))
                if tap == K * K - 1:
                    mm.then_inc(conv_ready, 1)

            def step(t, p):
                route_logits(t + 1)
                condconv_row(t, p, 0)
                group_mean(gmid, s_mid, ps_mid, t - 1)
                condconv_row(t, p, 1)
                group_var(gmid, s_mid, ps_mid, t - 1)
                condconv_row(t, p, 2)
                condconv_row(t, p, 3)
                for tap in range(K * K):
                    if has(t - 1):
                        sign_tap(t - 1, tap)
                    if tap == 4:
                        group_mean(gin, s_in, ps_in, t + 2)
                    if tap == 7:
                        group_var(gin, s_in, ps_in, t + 2)

            pe.wait_ge(zeroed, 2)
            pe.wait_ge(prm_loaded, 32)
            pe.wait_ge(ws_ready, 2)
            pipeline(pe, step)

        @block.scalar
        def _(act):
            def normalise(i):
                if has(i):
                    apart(act)
                    act.wait_ge(s_in["bias"], i + 1)
                    wait(act, v_ready, i)
                    nc.scalar.activation(xn[:, 1:1 + H, 1:1 + W],
                                         img(i).rearrange("p (h w) -> p h w", h=H), ACT.Identity,
                                         bias=gin["bias"][:, 0:1], scale=gin["rstd"][:, 0:1]).then_inc(xn_ready, 1)

            def tanh(i):
                if has(i):
                    act.wait_ge(logits_ready, i + 1)
                    nc.scalar.activation(th[:], logits[:], ACT.Tanh, scale=0.5).then_inc(tanh_ready, 1)

            def mix(i, p):
                if has(i):
                    act.wait_ge(route_ready, i + 1)
                    wait(act, m_ready, NU * (i - 1))
                    nc.scalar.activation(U[p][:].rearrange("p k n -> p (k n)"),
                                         UE[:, 0, :, :].rearrange("p k n -> p (k n)"), ACT.Copy,
                                         scale=route[:, 0:1]).then_inc(mix_first, 1)

            def split(i):
                if has(i):
                    apart(act)
                    act.wait_ge(s_mid["bias"], i + 1)
                    wait(act, lo_ready, i)
                    nc.scalar.activation(hn[:], img(i), ACT.Identity, bias=gmid["bias"][:, 0:1],
                                         scale=gmid["rstd"][:, 0:1]).then_inc(hn_ready, 1)
                    apart(act)
                    wait(act, conv_ready, i)
                    nc.scalar.activation(hi[:, 1:1 + H, 1:1 + W],
                                         img(i).rearrange("p (h w) -> p h w", h=H), ACT.Identity,
                                         bias=gmid["bias"][:, 0:1], scale=gmid["rstd"][:, 0:1]).then_inc(hi_ready, 1)

            def copy_m1(i):
                if has(i):
                    act.wait_ge(m_ready, NU * i + 1)
                    wait(act, m12_ready, 2 * i)
                    nc.scalar.copy(m1s[:], pm[1][:]).then_inc(m1_copied, 1)

            def silu(i):
                if has(i):
                    act.wait_ge(y_ready, 2 * i + 2)
                    nc.scalar.activation(y[:], y[:], ACT.Silu, bias=bn_shift[:, 0:1],
                                         scale=bn_scale[:, 0:1]).then_inc(silu_ready, 1)

            def step(t, p):
                tanh(t + 1)
                mix(t + 1, 1 - p)
                copy_m1(t)
                split(t - 1)
                silu(t)
                normalise(t + 2)

            act.wait_ge(zeroed, 7)
            act.wait_ge(bn_ready, 3)
            act.wait_ge(ue_ready, 1)
            pipeline(act, step)

        @block.vector
        def _(dve):
            v = nc.vector

            def stats(g, s, i):
                if has(i):
                    for half in range(2):
                        v.bn_stats(g["parts"][:, half, :], X[:, bass.ds(i * HW + half * BANK, BANK)])
                    dve.drain()
                    v.bn_aggr(g["mv"][:], g["parts"][:]).then_inc(s["mv"], 1)

            def spread(g, s, ps, i):
                if has(i):
                    dve.wait_ge(s["gmean"], i + 1)
                    v.tensor_tensor(g["dev"][:], g["mv"][:, 0:1], ps[:, MEAN], ALU.subtract).then_inc(s["dev"], 1)
                    dve.wait_ge(s["dev"], i + 1)
                    v.scalar_tensor_tensor(out=g["spread"][:], in0=g["dev"][:], scalar=g["dev"][:, 0:1],
                                           in1=g["mv"][:, 1:2], op0=ALU.mult, op1=ALU.add).then_inc(s["spread"], 1)

            def add_eps(g, s, ps, i, factor):
                if has(i):
                    dve.wait_ge(s["gvar"], i + 1)
                    v.tensor_scalar(g["ve"][:], ps[:, VAR], GN_EPS, factor, ALU.add, ALU.mult).then_inc(s["ve"], 1)

            def bias(g, s, ps, i):
                if has(i):
                    dve.wait_ge(s["rstd"], i + 1)
                    v.scalar_tensor_tensor(out=g["bias"][:], in0=ps[:, MEAN], scalar=-1.0, in1=g["rstd"][:],
                                           op0=ALU.mult, op1=ALU.mult).then_inc(s["bias"], 1)

            def pool_means(i):
                if has(i):
                    v.tensor_scalar(pooled[:], prm[:, P_WROUTE:P_WROUTE + E], gin["dev"][:, 0:1],
                                    gin["rstd"][:, 0:1], ALU.mult, ALU.mult).then_inc(pooled_ready, 1)

            def add_route_bias(i):
                if has(i):
                    dve.wait_ge(plogits_ready, i + 1)
                    v.tensor_tensor(logits[:], ps_in[:, LOG], prm[:, P_BROUTE:P_BROUTE + E], ALU.add) \
                     .then_inc(logits_ready, 1)

            def routing(i):
                if has(i):
                    dve.wait_ge(tanh_ready, i + 1)
                    v.tensor_scalar(route[:], th[:], 0.5, 0.5, ALU.mult, ALU.add).then_inc(route_ready, 1)

            def transform(i, p, k):
                if not has(i):
                    return
                if k == 0:
                    dve.wait_ge(xn_ready, i + 1)
                    wait(dve, m_ready, NU * (i - 1))
                a, b, op = ((0, 2, ALU.subtract), (1, 2, ALU.add), (2, 1, ALU.subtract), (1, 3, ALU.subtract))[k]
                ins = v.tensor_tensor(V[p][:, k, :, 1:1 + W], xn[:, a:a + H - 1:2, 1:1 + W],
                                      xn[:, b:b + H - 1:2, 1:1 + W], op)
                if k == NU - 1:
                    ins.then_inc(v_ready, 1)

            def mix(i, p, e):
                if has(i):
                    if e == 1:
                        dve.wait_ge(mix_first, i + 1)
                        dve.wait_ge(route_ready, i + 1)
                    else:
                        dve.wait_ge(mixed, (E - 1) * i + e - 1)
                    u = U[p][:].rearrange("p k n -> p (k n)")
                    v.scalar_tensor_tensor(out=u, in0=UE[:, e, :, :].rearrange("p k n -> p (k n)"),
                                           scalar=route[:, e:e + 1], in1=u, op0=ALU.mult, op1=ALU.add) \
                     .then_inc(mixed, 1)

            def low_part(i):
                if has(i):
                    dve.wait_ge(hn_ready, i + 1)
                    dve.wait_ge(hi_ready, i + 1)
                    wait(dve, conv_ready, i)
                    v.tensor_tensor(lo[:, 1:1 + H, 1:1 + W], hn[:].rearrange("p (h w) -> p h w", h=H),
                                    hi[:, 1:1 + H, 1:1 + W], ALU.subtract).then_inc(lo_ready, 1)

            def inverse(i):
                if has(i):
                    rows = y[:].rearrange("p (t two) w -> p two t w", two=2)
                    view = lambda ap: ap.rearrange("p (t w) -> p t w", t=TILES)
                    dve.wait_ge(m1_copied, i + 1)
                    dve.wait_ge(m_ready, NU * i + 2)
                    wait(dve, y_ready, 2 * i)
                    v.tensor_tensor(m12[:, 0, :], m1s[:], pm[2][:], ALU.add).then_inc(m12_ready, 1)
                    v.tensor_tensor(m12[:, 1, :], m1s[:], pm[2][:], ALU.subtract).then_inc(m12_ready, 1)
                    dve.wait_ge(m12_ready, 2 * i + 1)
                    dve.wait_ge(m_ready, NU * i + 3)
                    v.tensor_tensor(rows[:, 0, :, :], view(m12[:, 0, :]), view(pm[0][:]), ALU.add).then_inc(y_ready, 1)
                    dve.wait_ge(m12_ready, 2 * i + 2)
                    dve.wait_ge(m_ready, NU * i + 4)
                    v.tensor_tensor(rows[:, 1, :, :], view(m12[:, 1, :]), view(pm[3][:]), ALU.subtract) \
                     .then_inc(y_ready, 1)

            def residual(i):
                if has(i):
                    dve.wait_ge(silu_ready, i + 1)
                    v.tensor_tensor(img(i), img(i), y[:].rearrange("p h w -> p (h w)"), ALU.add).then_inc(h_ready, 1)

            def output(i):
                if has(i):
                    dve.wait_ge(conv_ready, i + 1)
                    v.scalar_tensor_tensor(out=img(i), in0=pc[:].rearrange("p a n -> p (a n)"),
                                           scalar=1.0 / ACT_SCALE, in1=img(i), op0=ALU.mult, op1=ALU.add) \
                     .then_inc(out_ready, 1)

            def step(t, p):
                output(t - 2)
                add_route_bias(t + 1)
                if has(t - 1):
                    apart(dve)
                    dve.wait_ge(h_ready, t)
                stats(gmid, s_mid, t - 1)
                routing(t + 1)
                transform(t + 1, 1 - p, 0)
                spread(gmid, s_mid, ps_mid, t - 1)
                transform(t + 1, 1 - p, 1)
                transform(t + 1, 1 - p, 2)
                add_eps(gmid, s_mid, ps_mid, t - 1, ACT_SCALE ** -2)
                transform(t + 1, 1 - p, 3)
                mix(t + 1, 1 - p, 1)
                bias(gmid, s_mid, ps_mid, t - 1)
                mix(t + 1, 1 - p, 2)
                low_part(t - 1)
                mix(t + 1, 1 - p, 3)
                if has(t + 2):
                    apart(dve)
                    if isinstance(t, int):
                        dve.wait_ge(x_loaded[p], 16 * ((t + 2) // 2 + 1))
                    else:
                        dve.wait_ge(x_loaded[p], 8 * (t - p + 2) + 16)
                stats(gin, s_in, t + 2)
                inverse(t)
                spread(gin, s_in, ps_in, t + 2)
                add_eps(gin, s_in, ps_in, t + 2, 1.0)
                residual(t)
                bias(gin, s_in, ps_in, t + 2)
                pool_means(t + 2)

            dve.wait_ge(prm_loaded, 32)
            v.tensor_scalar(bn_ve[:], prm[:, P_VAR:P_VAR + 1], BN_EPS, None, ALU.add).then_inc(bn_ve_ready, 1)
            dve.wait_ge(bn_rs_ready, 1)
            v.tensor_tensor(bn_scale[:], bn_rs[:], prm[:, P_GAMMA:P_GAMMA + 1], ALU.mult).then_inc(bn_ready, 1)
            dve.wait_ge(bn_ready, 1)
            v.tensor_tensor(bn_mscale[:], bn_scale[:], prm[:, P_MEAN:P_MEAN + 1], ALU.mult).then_inc(bn_ready, 1)
            dve.wait_ge(bn_ready, 2)
            v.tensor_tensor(bn_shift[:], prm[:, P_BETA:P_BETA + 1], bn_mscale[:], ALU.subtract).then_inc(bn_ready, 1)
            dve.wait_ge(zeroed, 7)

            for e in range(E):
                dve.wait_ge(we_loaded[e], 48)
                v.tensor_scalar(g1[:, e, :], g1[:, e, :], 0.5, None, ALU.mult).then_inc(ue_ready, 1)
                v.tensor_tensor(gsum[:, e, :], UE[:, e, 0, :], UE[:, e, 3, :], ALU.add).then_inc(ue_ready, 1)
                dve.wait_ge(ue_ready, 4 * e + 2)
                for k, op in ((1, ALU.add), (2, ALU.subtract)):
                    v.scalar_tensor_tensor(out=UE[:, e, k, :], in0=gsum[:, e, :], scalar=0.5, in1=g1[:, e, :],
                                           op0=ALU.mult, op1=op).then_inc(ue_ready, 1)
            dve.wait_ge(ue_ready, 4 * E)

            dve.wait_ge(ws_loaded, 16)
            v.tensor_scalar(ws_neg[:], ws_raw[:], 0.0, None, ALU.is_lt).then_inc(ws_ready, 1)
            dve.wait_ge(ws_ready, 1)
            v.scalar_tensor_tensor(out=ws[:], in0=ws_raw[:], scalar=0.0, in1=ws_neg[:], op0=ALU.is_gt,
                                   op1=ALU.subtract).then_inc(ws_ready, 1)
            pipeline(dve, step)


def kernel(x, L0_conv_w_route, L0_conv_b_route, L0_conv_w_experts, L0_conv_bn_gamma, L0_conv_bn_beta,
           L0_conv_bn_mean, L0_conv_bn_var, L1_conv_W):
    import concourse.bacc as bacc
    from concourse.bass_utils import run_bass_kernel_spmd

    lay = np.ascontiguousarray
    bn = [np.asarray(a)[:, None] for a in (L0_conv_bn_gamma, L0_conv_bn_beta, L0_conv_bn_mean, L0_conv_bn_var)]
    params = bn + [np.asarray(L0_conv_w_route).T, np.broadcast_to(np.asarray(L0_conv_b_route)[None, :], (C, E))]
    member = np.arange(C) // GSIZE
    arrays = {
        "x": lay(x),
        "w_experts": lay(np.transpose(np.asarray(L0_conv_w_experts), (2, 3, 0, 4, 1))),
        "w_sign": lay(np.transpose(np.asarray(L1_conv_W), (1, 2, 3, 0))),
        "params": lay(np.concatenate(params, axis=1)),
        "group_avg": ((member[:, None] == member[None, :]) / GSIZE).astype(np.float32),
    }
    nc = bacc.Bacc("TRN2", target_bir_lowering=False, num_devices=1)
    args = [nc.dram_tensor(n, a.shape, mybir.dt.from_np(a.dtype), kind="ExternalInput").ap() for n, a in arrays.items()]
    out = nc.dram_tensor("out", (B, C, H, W), F32, kind="ExternalOutput").ap()
    build(nc, *args, out)
    r = run_bass_kernel_spmd(nc, [arrays], core_ids=[0])
    return r.results[0]["out"]
```

```python
from contextlib import ExitStack

import numpy as np

import concourse.bass as bass
from concourse import mybir

F32 = mybir.dt.float32
F16 = mybir.dt.float16
ALU = mybir.AluOpType
ACT = mybir.ActivationFunctionType

B, C, H, W = 16, 128, 32, 32
E, K = 4, 3
HW = H * W
GROUPS = 32
GSIZE = C // GROUPS
PH, PW = H + 2, W + 2
TILES = H // 2
NU = 4
KCO = K * C
BANK = 512
GN_EPS = 1e-5
BN_EPS = 1e-5
ACT_SCALE = 256.0
MORDER = (1, 2, 0, 3)

P_GAMMA, P_BETA, P_MEAN, P_VAR, P_WROUTE, P_BROUTE, P_COLS = 0, 1, 2, 3, 4, 8, 12


def build(nc, x, w_experts, w_sign, params, group_avg, out):
    x_v = x.rearrange("b c h w -> b c (h w)")
    out_v = out.rearrange("b c h w -> b c (h w)")
    we_v = w_experts.rearrange("p k e x o -> p k e (x o)")
    ws_v = w_sign.rearrange("p y x o -> p (y x o)")

    with ExitStack() as ctx:
        def sb(name, shape, dt=F32):
            return ctx.enter_context(nc.sbuf_tensor(name, shape, dt))

        def psum(name, shape):
            return ctx.enter_context(nc.psum_tensor(name, shape, F32))

        def sem(name):
            return ctx.enter_context(nc.semaphore(name))

        X = sb("X", [C, B * HW])
        UE = sb("UE", [C, E, NU, KCO])
        g1 = sb("g1", [C, E, KCO])
        gsum = sb("gsum", [C, E, KCO])
        U = [sb(f"U{p}", [C, NU, KCO]) for p in range(2)]
        xn = sb("xn", [C, PH, PW])
        V = [sb(f"V{p}", [C, NU, TILES, PW]) for p in range(2)]
        m1s = sb("m1s", [C, BANK])
        m12 = sb("m12", [C, 2, BANK])
        y = sb("y", [C, H, W])
        hn = sb("hn", [C, HW])
        hi = sb("hi", [C, PH, PW], F16)
        lo = sb("lo", [C, PH, PW], F16)
        ws_raw = sb("ws_raw", [C, K * KCO])
        ws_neg = sb("ws_neg", [C, K * KCO], F16)
        ws = sb("ws", [C, K * KCO], F16)
        prm = sb("prm", [C, P_COLS])
        gavg = sb("gavg", [C, 2, C])
        ones = sb("ones", [C, C])
        nhalf = sb("nhalf", [C, 1])
        bn_ve = sb("bn_ve", [C, 1])
        bn_rs = sb("bn_rs", [C, 1])
        bn_scale = sb("bn_scale", [C, 1])
        bn_mscale = sb("bn_mscale", [C, 1])
        bn_shift = sb("bn_shift", [C, 1])

        def chain(tag):
            names = ("mean", "nmean", "var", "dev", "spread", "ve", "rstd", "bias")
            return {n: sb(f"{n}_{tag}", [C, 1]) for n in names}

        gin, gmid = chain("in"), chain("mid")
        pooled = sb("pooled", [C, E])
        bshare = sb("bshare", [C, E])
        npooled = sb("npooled", [C, 1])
        junk = sb("junk", [C, HW])
        th = sb("th", [C, E])
        hsum = sb("hsum", [C, 1])
        route = sb("route", [C, E])

        pm = [psum(f"pm{k}", [C, BANK]) for k in range(NU)]
        pc = psum("pc", [C, 2, BANK])
        ps_in = psum("ps_in", [C, BANK])
        ps_mid = psum("ps_mid", [C, BANK])
        MEAN, VAR, LOG = slice(0, 1), slice(1, 2), slice(2, 2 + E)

        x_loaded = [sem("x_loaded0"), sem("x_loaded1")]
        we_loaded = [sem(f"we_loaded{e}") for e in range(E)]
        ws_loaded = sem("ws_loaded")
        prm_loaded = sem("prm_loaded")
        stored = sem("stored")
        zeroed = sem("zeroed")
        bn_ve_ready = sem("bn_ve_ready")
        bn_rs_ready = sem("bn_rs_ready")
        bn_ready = sem("bn_ready")
        ue_ready = sem("ue_ready")
        ws_ready = sem("ws_ready")

        def chain_sems(tag):
            names = ("mean", "nmean", "var", "gmean", "dev", "spread", "gvar", "ve", "rstd", "bias")
            return {n: sem(f"{n}_{tag}_ready") for n in names}

        s_in, s_mid = chain_sems("in"), chain_sems("mid")
        pooled_ready = sem("pooled_ready")
        plogits_ready = sem("plogits_ready")
        npooled_ready = sem("npooled_ready")
        bshare_ready = sem("bshare_ready")
        tanh_ready = sem("tanh_ready")
        route_ready = sem("route_ready")
        xn_ready = sem("xn_ready")
        v_ready = sem("v_ready")
        mix_first = sem("mix_first")
        mixed = sem("mixed")
        m_ready = sem("m_ready")
        m1_copied = sem("m1_copied")
        m12_ready = sem("m12_ready")
        y_ready = sem("y_ready")
        silu_ready = sem("silu_ready")
        h_ready = sem("h_ready")
        hn_ready = sem("hn_ready")
        hi_ready = sem("hi_ready")
        lo_ready = sem("lo_ready")
        conv_ready = sem("conv_ready")
        out_ready = sem("out_ready")

        def img(i):
            return X[:, bass.ts(i, HW)]

        def has(i):
            return not isinstance(i, int) or 0 <= i < B

        def wait(eng, s, n):
            if not isinstance(n, int) or n > 0:
                eng.wait_ge(s, n)

        def at(i, n):
            return isinstance(i, int) and i == n

        def apart(eng):
            eng.wait_ge(prm_loaded, 32)

        def pipeline(eng, step, after=None):
            lo_t, hi_t = 2, B - 2
            for t in range(-2, lo_t):
                step(t, t % 2)
                if after and t == -1:
                    after()
            with eng.Fori(lo_t, hi_t - 1, 2) as t:
                step(t, 0)
                step(t + 1, 1)
            for t in range(hi_t, B + 2):
                step(t, t % 2)

        block = ctx.enter_context(nc.Block())

        @block.sync
        def _(sp):
            def load(i, p):
                sp.dma_start(img(i), x_v[i, :, :]).then_inc(x_loaded[p], 16)

            load(0, 0)
            sp.dma_start(prm[:], params).then_inc(prm_loaded, 16)
            sp.dma_start(gavg[:], group_avg).then_inc(prm_loaded, 16)
            for e in range(E):
                sp.dma_start(UE[:, e, 0, :], we_v[:, 0, e, :]).then_inc(we_loaded[e], 16)
                sp.dma_start(UE[:, e, NU - 1, :], we_v[:, 2, e, :]).then_inc(we_loaded[e], 16)
                sp.dma_start(g1[:, e, :], we_v[:, 1, e, :]).then_inc(we_loaded[e], 16)
            load(1, 1)
            sp.dma_start(ws_raw[:], ws_v).then_inc(ws_loaded, 16)
            with sp.Fori(2, B - 1, 2) as i:
                for p in range(2):
                    sp.wait_ge(x_loaded[p], i * 8)
                    load(i + p, p)
            with sp.Fori(0, B) as i:
                sp.wait_ge(out_ready, i + 1)
                sp.dma_start(out_v[i, :, :], img(i)).then_inc(stored, 16)
            sp.wait_ge(stored, 16 * B)

        @block.gpsimd
        def _(pool):
            nc.gpsimd.memset(nhalf[:], -0.5).then_inc(zeroed, 1)
            nc.gpsimd.memset(ones[:], 1.0).then_inc(zeroed, 1)
            nc.gpsimd.memset(xn[:], 0.0).then_inc(zeroed, 1)
            for p in range(2):
                nc.gpsimd.memset(V[p][:], 0.0).then_inc(zeroed, 1)
            nc.gpsimd.memset(hi[:], 0.0).then_inc(zeroed, 1)
            nc.gpsimd.memset(lo[:], 0.0).then_inc(zeroed, 1)
            pool.wait_ge(zeroed, 1)
            pool.wait_ge(bn_ve_ready, 1)
            nc.gpsimd.tensor_tensor(bn_rs[:], bn_ve[:], nhalf[:], ALU.pow).then_inc(bn_rs_ready, 1)

            def power(g, s, i):
                if has(i):
                    pool.wait_ge(s["ve"], i + 1)
                    nc.gpsimd.tensor_tensor(g["rstd"][:], g["ve"][:], nhalf[:], ALU.pow).then_inc(s["rstd"], 1)

            def step(t, p):
                power(gmid, s_mid, t - 1)
                power(gin, s_in, t + 2)

            pipeline(pool, step)

        @block.tensor
        def _(pe):
            def group_mean(g, s, ps, i):
                if has(i):
                    pe.wait_ge(s["mean"], i + 1)
                    nc.tensor.matmul(ps[:, MEAN], gavg[:, 0, :], g["mean"][:], start=True, stop=True) \
                      .then_inc(s["gmean"], 1)

            def group_var(g, s, ps, i):
                if has(i):
                    pe.wait_ge(s["spread"], i + 1)
                    nc.tensor.matmul(ps[:, VAR], gavg[:, 1, :], g["spread"][:], start=True, stop=True) \
                      .then_inc(s["gvar"], 1)

            def route_logits(i):
                if has(i):
                    pe.wait_ge(pooled_ready, i + 1)
                    nc.tensor.matmul(ps_in[:, LOG], ones[:], pooled[:], start=True, stop=True) \
                      .then_inc(plogits_ready, 1)

            def condconv_row(t, p, n):
                if not has(t):
                    return
                k = MORDER[n]
                if n == 0:
                    pe.wait_ge(v_ready, t + 1)
                    pe.wait_ge(mixed, (E - 1) * (t + 1))
                if k == 1:
                    wait(pe, m1_copied, t)
                elif k == 2:
                    wait(pe, m12_ready, 2 * t)
                else:
                    wait(pe, y_ready, 2 * t - (1 if k == 0 else 0))
                for kx in range(K):
                    mm = nc.tensor.matmul(pm[k][:], U[p][:, k, kx * C:(kx + 1) * C],
                                          V[p][:, k, :, kx:kx + W], start=(kx == 0), stop=(kx == K - 1))
                mm.then_inc(m_ready, 1)

            def sign_tap(i, tap):
                ky, kx = tap // K, tap % K
                if tap == 0:
                    pe.wait_ge(hi_ready, i + 1)
                    pe.wait_ge(lo_ready, i + 1)
                    wait(pe, out_ready, i)
                for part in (hi, lo):
                    for half in range(2):
                        r = half * (H // 2) + ky
                        mm = nc.tensor.matmul(pc[:, half, :], ws[:, tap * C:(tap + 1) * C],
                                              part[:, r:r + H // 2, kx:kx + W],
                                              start=(tap == 0 and part is hi),
                                              stop=(tap == K * K - 1 and part is lo))
                if tap == K * K - 1:
                    mm.then_inc(conv_ready, 1)

            def step(t, p):
                route_logits(t + 1)
                for n in range(NU):
                    condconv_row(t, p, n)
                if at(t, 1):
                    pe.wait_ge(ws_ready, 2)
                for tap in range(K * K):
                    if tap == 0:
                        group_mean(gin, s_in, ps_in, t + 2)
                    if tap == 2:
                        group_var(gin, s_in, ps_in, t + 2)
                    if tap == 5:
                        group_mean(gmid, s_mid, ps_mid, t)
                    if tap == 8:
                        group_var(gmid, s_mid, ps_mid, t)
                    if has(t - 1):
                        sign_tap(t - 1, tap)

            pe.wait_ge(zeroed, 2)
            pe.wait_ge(prm_loaded, 32)
            pipeline(pe, step)

        @block.scalar
        def _(act):
            def stats_in(i, p):
                if has(i):
                    apart(act)
                    act.wait_ge(x_loaded[p], 16 * (i // 2 + 1) if isinstance(i, int) else 8 * (i - p) + 16)
                    nc.scalar.activation(junk[:], img(i), ACT.Identity, scale=1.0 / HW,
                                         accum_out=gin["mean"][:]).then_inc(s_in["mean"], 1)
                    channel_var(gin, s_in, i)

            def channel_var(g, s, i):
                if has(i):
                    act.wait_ge(s["mean"], i + 1)
                    nc.scalar.activation(g["nmean"][:], g["mean"][:], ACT.Copy, scale=-HW ** -0.5).then_inc(s["nmean"], 1)
                    apart(act)
                    act.wait_ge(s["nmean"], i + 1)
                    nc.scalar.activation(junk[:], img(i), ACT.Square, bias=g["nmean"][:, 0:1], scale=HW ** -0.5,
                                         accum_out=g["var"][:]).then_inc(s["var"], 1)

            def spread(g, s, ps, i):
                if has(i):
                    act.wait_ge(s["gmean"], i + 1)
                    nc.scalar.activation(g["dev"][:], ps[:, MEAN], ACT.Identity, bias=g["mean"][:, 0:1]) \
                      .then_inc(s["dev"], 1)
                    act.wait_ge(s["dev"], i + 1)
                    act.wait_ge(s["var"], i + 1)
                    nc.scalar.activation(g["spread"][:], g["dev"][:], ACT.Identity, bias=g["var"][:, 0:1],
                                         scale=g["dev"][:, 0:1]).then_inc(s["spread"], 1)

            def add_eps(g, s, ps, i, factor):
                if has(i):
                    act.wait_ge(s["gvar"], i + 1)
                    nc.scalar.activation(g["ve"][:], ps[:, VAR], ACT.Copy, bias=GN_EPS * factor, scale=factor) \
                      .then_inc(s["ve"], 1)

            def bias(g, s, ps, i):
                if has(i):
                    act.wait_ge(s["rstd"], i + 1)
                    nc.scalar.activation(g["bias"][:], ps[:, MEAN], ACT.Copy, scale=g["rstd"][:, 0:1]) \
                      .then_inc(s["bias"], 1)

            def normalise(i):
                if has(i):
                    nc.scalar.activation(npooled[:], gin["dev"][:], ACT.Copy, scale=gin["rstd"][:, 0:1]) \
                      .then_inc(npooled_ready, 1)
                    apart(act)
                    act.wait_ge(s_in["bias"], i + 1)
                    wait(act, v_ready, i)
                    nc.scalar.activation(xn[:, 1:1 + H, 1:1 + W],
                                         img(i).rearrange("p (h w) -> p h w", h=H), ACT.Identity,
                                         bias=gin["bias"][:, 0:1], scale=gin["rstd"][:, 0:1]).then_inc(xn_ready, 1)

            def routing(i):
                if has(i):
                    act.wait_ge(plogits_ready, i + 1)
                    nc.scalar.activation(th[:], ps_in[:, LOG], ACT.Tanh, scale=0.5).then_inc(tanh_ready, 1)
                    act.wait_ge(tanh_ready, i + 1)
                    wait(act, mixed, (E - 1) * i)
                    nc.scalar.activation(route[:], th[:], ACT.Copy, bias=0.5, scale=0.5).then_inc(route_ready, 1)

            def mix(i, p):
                if has(i):
                    act.wait_ge(route_ready, i + 1)
                    if at(i, 0):
                        act.wait_ge(ue_ready, 4)
                    wait(act, m_ready, NU * (i - 1))
                    nc.scalar.activation(U[p][:].rearrange("p k n -> p (k n)"),
                                         UE[:, 0, :, :].rearrange("p k n -> p (k n)"), ACT.Copy,
                                         scale=route[:, 0:1]).then_inc(mix_first, 1)

            def split(i):
                if has(i):
                    apart(act)
                    act.wait_ge(s_mid["bias"], i + 1)
                    wait(act, lo_ready, i)
                    nc.scalar.activation(hn[:], img(i), ACT.Identity, bias=gmid["bias"][:, 0:1],
                                         scale=gmid["rstd"][:, 0:1]).then_inc(hn_ready, 1)
                    apart(act)
                    wait(act, conv_ready, i)
                    nc.scalar.activation(hi[:, 1:1 + H, 1:1 + W],
                                         img(i).rearrange("p (h w) -> p h w", h=H), ACT.Identity,
                                         bias=gmid["bias"][:, 0:1], scale=gmid["rstd"][:, 0:1]).then_inc(hi_ready, 1)

            def copy_m1(i):
                if has(i):
                    act.wait_ge(m_ready, NU * i + 1)
                    wait(act, m12_ready, 2 * i)
                    nc.scalar.copy(m1s[:], pm[1][:]).then_inc(m1_copied, 1)

            def silu(i):
                if has(i):
                    act.wait_ge(y_ready, 2 * i + 2)
                    nc.scalar.activation(y[:], y[:], ACT.Silu, bias=bn_shift[:, 0:1],
                                         scale=bn_scale[:, 0:1]).then_inc(silu_ready, 1)

            def step(t, p):
                routing(t + 1)
                mix(t + 1, 1 - p)
                copy_m1(t)
                bias(gmid, s_mid, ps_mid, t - 1)
                split(t - 1)
                stats_in(t + 2, p)
                spread(gin, s_in, ps_in, t + 2)
                silu(t)
                add_eps(gin, s_in, ps_in, t + 2, 1.0)
                bias(gin, s_in, ps_in, t + 2)
                normalise(t + 2)
                channel_var(gmid, s_mid, t)
                spread(gmid, s_mid, ps_mid, t)
                add_eps(gmid, s_mid, ps_mid, t, ACT_SCALE ** -2)

            def after():
                act.wait_ge(bn_ready, 3)

            act.wait_ge(zeroed, 7)
            pipeline(act, step, after)

        @block.vector
        def _(dve):
            v = nc.vector

            def route_products(i):
                if has(i):
                    dve.wait_ge(npooled_ready, i + 1)
                    v.scalar_tensor_tensor(out=pooled[:], in0=prm[:, P_WROUTE:P_WROUTE + E], scalar=npooled[:, 0:1],
                                           in1=bshare[:], op0=ALU.mult, op1=ALU.add).then_inc(pooled_ready, 1)

            def expert(e):
                dve.wait_ge(we_loaded[e], 48)
                v.tensor_scalar(g1[:, e, :], g1[:, e, :], 0.5, None, ALU.mult).then_inc(ue_ready, 1)
                v.tensor_tensor(gsum[:, e, :], UE[:, e, 0, :], UE[:, e, 3, :], ALU.add).then_inc(ue_ready, 1)
                dve.wait_ge(ue_ready, 4 * e + 2)
                for k, op in ((1, ALU.add), (2, ALU.subtract)):
                    v.scalar_tensor_tensor(out=UE[:, e, k, :], in0=gsum[:, e, :], scalar=0.5, in1=g1[:, e, :],
                                           op0=ALU.mult, op1=op).then_inc(ue_ready, 1)

            def transform(i, p, k):
                if not has(i):
                    return
                if k == 0:
                    dve.wait_ge(xn_ready, i + 1)
                    wait(dve, m_ready, NU * (i - 1))
                a, b, op = ((0, 2, ALU.subtract), (1, 2, ALU.add), (2, 1, ALU.subtract), (1, 3, ALU.subtract))[k]
                ins = v.tensor_tensor(V[p][:, k, :, 1:1 + W], xn[:, a:a + H - 1:2, 1:1 + W],
                                      xn[:, b:b + H - 1:2, 1:1 + W], op)
                if k == NU - 1:
                    ins.then_inc(v_ready, 1)

            def mix(i, p, e):
                if has(i):
                    if at(i, 0):
                        expert(e)
                        dve.wait_ge(ue_ready, 4 * e + 4)
                    if e == 1:
                        dve.wait_ge(mix_first, i + 1)
                        dve.wait_ge(route_ready, i + 1)
                    else:
                        dve.wait_ge(mixed, (E - 1) * i + e - 1)
                    u = U[p][:].rearrange("p k n -> p (k n)")
                    v.scalar_tensor_tensor(out=u, in0=UE[:, e, :, :].rearrange("p k n -> p (k n)"),
                                           scalar=route[:, e:e + 1], in1=u, op0=ALU.mult, op1=ALU.add) \
                     .then_inc(mixed, 1)

            def low_part(i):
                if has(i):
                    dve.wait_ge(hn_ready, i + 1)
                    dve.wait_ge(hi_ready, i + 1)
                    wait(dve, conv_ready, i)
                    v.tensor_tensor(lo[:, 1:1 + H, 1:1 + W], hn[:].rearrange("p (h w) -> p h w", h=H),
                                    hi[:, 1:1 + H, 1:1 + W], ALU.subtract).then_inc(lo_ready, 1)

            def inverse(i, part):
                if not has(i):
                    return
                rows = y[:].rearrange("p (t two) w -> p two t w", two=2)
                view = lambda ap: ap.rearrange("p (t w) -> p t w", t=TILES)
                if part == 0:
                    dve.wait_ge(m1_copied, i + 1)
                    dve.wait_ge(m_ready, NU * i + 2)
                    wait(dve, y_ready, 2 * i)
                    v.tensor_tensor(m12[:, 0, :], m1s[:], pm[2][:], ALU.add).then_inc(m12_ready, 1)
                    v.tensor_tensor(m12[:, 1, :], m1s[:], pm[2][:], ALU.subtract).then_inc(m12_ready, 1)
                elif part == 1:
                    dve.wait_ge(m12_ready, 2 * i + 1)
                    dve.wait_ge(m_ready, NU * i + 3)
                    v.tensor_tensor(rows[:, 0, :, :], view(m12[:, 0, :]), view(pm[0][:]), ALU.add).then_inc(y_ready, 1)
                else:
                    dve.wait_ge(m12_ready, 2 * i + 2)
                    dve.wait_ge(m_ready, NU * i + 4)
                    v.tensor_tensor(rows[:, 1, :, :], view(m12[:, 1, :]), view(pm[3][:]), ALU.subtract) \
                     .then_inc(y_ready, 1)

            def residual(i):
                if has(i):
                    dve.wait_ge(silu_ready, i + 1)
                    v.scalar_tensor_tensor(out=img(i), in0=y[:].rearrange("p h w -> p (h w)"), scalar=1.0, in1=img(i),
                                           op0=ALU.mult, op1=ALU.add, accum_out=hsum[:]).then_inc(h_ready, 1)
                    dve.wait_ge(h_ready, i + 1)
                    v.tensor_scalar(gmid["mean"][:], hsum[:], 1.0 / HW, None, ALU.mult).then_inc(s_mid["mean"], 1)

            def output(i):
                if has(i):
                    dve.wait_ge(conv_ready, i + 1)
                    v.scalar_tensor_tensor(out=img(i), in0=pc[:].rearrange("p a n -> p (a n)"),
                                           scalar=1.0 / ACT_SCALE, in1=img(i), op0=ALU.mult, op1=ALU.add) \
                     .then_inc(out_ready, 1)

            def step(t, p):
                output(t - 2)
                if at(t, -1):
                    expert(0)
                for k in range(NU):
                    transform(t + 1, 1 - p, k)
                mix(t + 1, 1 - p, 1)
                inverse(t, 0)
                low_part(t - 1)
                inverse(t, 1)
                mix(t + 1, 1 - p, 2)
                inverse(t, 2)
                mix(t + 1, 1 - p, 3)
                residual(t)
                route_products(t + 2)

            def after():
                dve.wait_ge(bn_rs_ready, 1)
                v.tensor_tensor(bn_scale[:], bn_rs[:], prm[:, P_GAMMA:P_GAMMA + 1], ALU.mult).then_inc(bn_ready, 1)
                dve.wait_ge(bn_ready, 1)
                v.tensor_tensor(bn_mscale[:], bn_scale[:], prm[:, P_MEAN:P_MEAN + 1], ALU.mult).then_inc(bn_ready, 1)
                dve.wait_ge(bn_ready, 2)
                v.tensor_tensor(bn_shift[:], prm[:, P_BETA:P_BETA + 1], bn_mscale[:], ALU.subtract).then_inc(bn_ready, 1)
                dve.wait_ge(ws_loaded, 16)
                v.tensor_scalar(ws_neg[:], ws_raw[:], 0.0, None, ALU.is_lt).then_inc(ws_ready, 1)
                dve.wait_ge(ws_ready, 1)
                v.scalar_tensor_tensor(out=ws[:], in0=ws_raw[:], scalar=0.0, in1=ws_neg[:], op0=ALU.is_gt,
                                       op1=ALU.subtract).then_inc(ws_ready, 1)

            dve.wait_ge(prm_loaded, 32)
            v.tensor_scalar(bn_ve[:], prm[:, P_VAR:P_VAR + 1], BN_EPS, None, ALU.add).then_inc(bn_ve_ready, 1)
            v.tensor_scalar(bshare[:], prm[:, P_BROUTE:P_BROUTE + E], 1.0 / C, None, ALU.mult).then_inc(bshare_ready, 1)
            dve.wait_ge(bshare_ready, 1)
            dve.wait_ge(zeroed, 7)
            pipeline(dve, step, after)


def kernel(x, L0_conv_w_route, L0_conv_b_route, L0_conv_w_experts, L0_conv_bn_gamma, L0_conv_bn_beta,
           L0_conv_bn_mean, L0_conv_bn_var, L1_conv_W):
    import concourse.bacc as bacc
    from concourse.bass_utils import run_bass_kernel_spmd

    lay = np.ascontiguousarray
    bn = [np.asarray(a)[:, None] for a in (L0_conv_bn_gamma, L0_conv_bn_beta, L0_conv_bn_mean, L0_conv_bn_var)]
    params = bn + [np.asarray(L0_conv_w_route).T, np.broadcast_to(np.asarray(L0_conv_b_route)[None, :], (C, E))]
    member = np.arange(C) // GSIZE
    within = (member[:, None] == member[None, :]).astype(np.float32) / GSIZE
    group_avg = np.stack([-within, within], axis=1)
    arrays = {
        "x": lay(x),
        "w_experts": lay(np.transpose(np.asarray(L0_conv_w_experts), (2, 3, 0, 4, 1))),
        "w_sign": lay(np.transpose(np.asarray(L1_conv_W), (1, 2, 3, 0))),
        "params": lay(np.concatenate(params, axis=1)),
        "group_avg": group_avg,
    }
    nc = bacc.Bacc("TRN2", target_bir_lowering=False, num_devices=1)
    args = [nc.dram_tensor(n, a.shape, mybir.dt.from_np(a.dtype), kind="ExternalInput").ap() for n, a in arrays.items()]
    out = nc.dram_tensor("out", (B, C, H, W), F32, kind="ExternalOutput").ap()
    build(nc, *args, out)
    r = run_bass_kernel_spmd(nc, [arrays], core_ids=[0])
    return r.results[0]["out"]
```

```python
from contextlib import ExitStack

import numpy as np

import concourse.bass as bass
from concourse import mybir

F32 = mybir.dt.float32
F16 = mybir.dt.float16
ALU = mybir.AluOpType
ACT = mybir.ActivationFunctionType
AX_X = mybir.AxisListType.X

B, C, H, W = 16, 128, 32, 32
E, K = 4, 3
HW = H * W
GROUPS = 32
GSIZE = C // GROUPS
PH, PW = H + 2, W + 2
TILES = H // 2
NU = 4
KCO = K * C
BANK = 512
GN_EPS = 1e-5
BN_EPS = 1e-5
ACT_SCALE = 256.0
MORDER = (0, 2, 1, 3)
G0, G2, G1 = 0, 1, 2
SLOT = (0, 2, 3, 1)
EARLY = 2
LATE = 2
IN, MID = 0, 1
SQ = 32
SG = SQ // GSIZE
WARM = (9, 8)

P_GAMMA, P_BETA, P_MEAN, P_VAR, P_WROUTE, P_BROUTE, P_COLS = 0, 1, 2, 3, 4, 8, 12


def build(nc, x, w_experts, w_sign, params, out):
    x_v = x.rearrange("b c h w -> b c (h w)")
    out_v = out.rearrange("b c h w -> b c (h w)")
    we_v = w_experts.rearrange("p k e x o -> p k e (x o)")
    x_halves = x.rearrange("b c (s h) w -> b s c (h w)", s=2)
    ws_v = w_sign.rearrange("p y x o -> p (y x o)")

    with ExitStack() as ctx:
        def sb(name, shape, dt=F32):
            return ctx.enter_context(nc.sbuf_tensor(name, shape, dt))

        def psum(name, shape):
            return ctx.enter_context(nc.psum_tensor(name, shape, F32))

        def sem(name):
            return ctx.enter_context(nc.semaphore(name))

        X = sb("X", [C, B * HW])
        we = sb("we", [C, E, K, KCO])
        U = [sb(f"U{p}", [C, NU, KCO]) for p in range(2)]
        g02 = sb("g02", [C, KCO])
        scaled = sb("scaled", [C, E - 1, KCO])
        xn = sb("xn", [C, PH, PW])
        V = [sb(f"V{p}", [C, NU, TILES, PW]) for p in range(2)]
        m2s = sb("m2s", [C, BANK])
        m12 = sb("m12", [C, 2, BANK])
        y = sb("y", [C, H, W])
        hn = sb("hn", [C, HW])
        hi = [sb(f"hi{p}", [C, PH, PW], F16) for p in range(2)]
        lo = [sb(f"lo{p}", [C, PH, PW], F16) for p in range(2)]
        ws_raw = sb("ws_raw", [C, K * KCO])
        ws_pos = sb("ws_pos", [C, K * KCO], F16)
        ws_neg = sb("ws_neg", [C, K * KCO], F16)
        ws = sb("ws", [C, K * KCO], F16)
        prm = sb("prm", [C, P_COLS])
        ones = sb("ones", [C, C])
        nhalf = sb("nhalf", [C, 2])
        bn_ve = sb("bn_ve", [C, 1])
        bn_rs = sb("bn_rs", [C, 1])
        bn_scale = sb("bn_scale", [C, 1])
        bn_mscale = sb("bn_mscale", [C, 1])
        bn_shift = sb("bn_shift", [C, 1])

        stat = sb("stat", [C, 2 * SQ])
        halves = sb("halves", [C, 2, 6])
        nmean = sb("nmean", [C, 2])
        statT = sb("statT", [C, 2 * SQ])
        gsumT = sb("gsumT", [C, SG])
        dev2T = sb("dev2T", [C, SQ])
        spreadT = sb("spreadT", [C, SQ])
        gspreadT = sb("gspreadT", [C, SG])
        normT = sb("normT", [C, 3 * SQ])
        norm = sb("norm", [C, 3 * SQ])
        rstd = sb("rstd", [C, 2])
        gbias = sb("gbias", [C, 2])
        mean, var = stat[:, 0:2], stat[:, SQ:SQ + 2]
        ve, ngmean, dev_in = norm[:, 0:2], norm[:, SQ:SQ + 2], norm[:, 2 * SQ + IN:2 * SQ + IN + 1]
        contrib = sb("contrib", [C, E])
        pooled = sb("pooled", [C, E])
        bshare = sb("bshare", [C, E])
        wroute = sb("wroute", [C, E])
        junk = sb("junk", [C, HW])
        th = sb("th", [C, E])
        warm_out = sb("warm_out", [C, 1])
        hsum = sb("hsum", [C, 1])
        route = [sb(f"route{p}", [C, E]) for p in range(2)]

        pm = [psum(f"pm{k}", [C, BANK]) for k in range(NU)]
        pc = psum("pc", [C, 2, BANK])
        ps_route = psum("ps_route", [C, BANK])
        ps_warm = psum("ps_warm", [C, BANK])
        ps_logits = ps_route[:, 0:E]

        x_loaded = [sem("x_loaded0"), sem("x_loaded1")]
        x_half_loaded = sem("x_half_loaded")
        we_loaded = [sem(f"we_loaded{g}") for g in range(K)]
        ws_loaded = sem("ws_loaded")
        prm_loaded = sem("prm_loaded")
        stored = sem("stored")
        zeroed = sem("zeroed")
        bn_ve_ready = sem("bn_ve_ready")
        bn_rs_ready = sem("bn_rs_ready")
        bn_ready = sem("bn_ready")
        ws_ready = sem("ws_ready")

        mean_in_ready = sem("mean_in_ready")
        mean_mid_ready = sem("mean_mid_ready")
        nmean_in_ready = sem("nmean_in_ready")
        nmean_mid_ready = sem("nmean_mid_ready")
        var_in_ready = sem("var_in_ready")
        var_mid_ready = sem("var_mid_ready")
        statT_ready = sem("statT_ready")
        gsumT_ready = sem("gsumT_ready")
        dev2T_ready = sem("dev2T_ready")
        spreadT_ready = sem("spreadT_ready")
        gspreadT_ready = sem("gspreadT_ready")
        normT_ready = sem("normT_ready")
        norm_ready = sem("norm_ready")
        rstd_ready = sem("rstd_ready")
        gbias_ready = sem("gbias_ready")
        contrib_ready = sem("contrib_ready")
        pooled_ready = sem("pooled_ready")
        plogits_ready = sem("plogits_ready")
        route_prm_ready = sem("route_prm_ready")
        tanh_ready = sem("tanh_ready")
        route_ready = sem("route_ready")
        xn_ready = sem("xn_ready")
        scaled_ready = sem("scaled_ready")
        summed = sem("summed")
        v_pool_ready = sem("v_pool_ready")
        v_ready = sem("v_ready")
        mix_first = sem("mix_first")
        mixed = sem("mixed")
        kernel_ready = sem("kernel_ready")
        m_ready = sem("m_ready")
        m2_copied = sem("m2_copied")
        m12_ready = sem("m12_ready")
        y_ready = sem("y_ready")
        silu_ready = sem("silu_ready")
        h_ready = sem("h_ready")
        hn_ready = sem("hn_ready")
        hi_ready = sem("hi_ready")
        lo_ready = sem("lo_ready")
        conv_ready = sem("conv_ready")
        out_ready = sem("out_ready")

        def img(i):
            return X[:, bass.ts(i, HW)]

        def has(i):
            return not isinstance(i, int) or 0 <= i < B

        def wait(eng, s, n):
            if not isinstance(n, int) or n > 0:
                eng.wait_ge(s, n)

        def at(i, n):
            return isinstance(i, int) and i == n

        def apart(eng):
            eng.wait_ge(prm_loaded, 16)

        def chained(t):
            return has(t + 2) or has(t)

        def is_early(i):
            return isinstance(i, int) and i < EARLY

        def mixed_before(i):
            return (E - 1) * (2 * i if is_early(i) else i + EARLY)

        def out_parts(i):
            if i == B - 1:
                return ((BANK, BANK + BANK // 2), (0, BANK), (BANK + BANK // 2, HW))
            return ((0, BANK), (BANK, HW))

        def conv_psum(first, last):
            bank = first // BANK
            if last - first < BANK and last == HW:
                return pm[0][:, 0:last - first]
            return pc[:, bank, first - bank * BANK:last - bank * BANK]

        def sums_before(i):
            if isinstance(i, int) and i > B - LATE:
                return B - LATE + sum(len(out_parts(j)) for j in range(B - LATE, i))
            return i

        def transform_rows(k):
            return ((0, 2, ALU.subtract), (1, 2, ALU.add), (2, 1, ALU.subtract), (1, 3, ALU.subtract))[k]

        def pipeline(eng, step):
            lo_t, hi_t = 2, B - 2
            for t in range(-2, lo_t):
                step(t, t % 2)
            with eng.Fori(lo_t, hi_t - 1, 2) as t:
                step(t, 0)
                step(t + 1, 1)
            for t in range(hi_t, B + 2):
                step(t, t % 2)

        block = ctx.enter_context(nc.Block())

        @block.sync
        def _(sp):
            def load(i, p):
                sp.dma_start(img(i), x_v[i, :, :]).then_inc(x_loaded[p], 16)

            sp.dma_start(img(0)[:, 0:BANK], x_halves[0, 0, :, :]).then_inc(x_half_loaded, 16)
            sp.dma_start(img(0)[:, BANK:HW], x_halves[0, 1, :, :]).then_inc(x_loaded[0], 16)
            sp.dma_start(prm[:], params).then_inc(prm_loaded, 16)
            for slot, row in ((G0, 0), (G2, 2), (G1, 1)):
                sp.dma_start(we[:, :, slot, :], we_v[:, row, :, :]).then_inc(we_loaded[slot], 16)
            load(1, 1)
            sp.dma_start(ws_raw[:], ws_v).then_inc(ws_loaded, 16)
            with sp.Fori(2, B - 1, 2) as i:
                for p in range(2):
                    sp.wait_ge(x_loaded[p], i * 8)
                    load(i + p, p)
            with sp.Fori(0, B - LATE) as i:
                sp.wait_ge(out_ready, i + 1)
                sp.dma_start(out_v[i, :, :], img(i)).then_inc(stored, 16)
            for i in range(B - LATE, B):
                for n, (first, last) in enumerate(out_parts(i)):
                    sp.wait_ge(out_ready, sums_before(i) + n + 1)
                    sp.dma_start(out_v[i, :, first:last], img(i)[:, first:last]).then_inc(stored, 16)
            sp.wait_ge(stored, 16 * sums_before(B))

        @block.gpsimd
        def _(pool):
            nc.gpsimd.memset(nhalf[:], -0.5).then_inc(zeroed, 1)
            nc.gpsimd.memset(ones[:], 1.0).then_inc(zeroed, 1)
            for buf in (xn, *hi, *lo):
                nc.gpsimd.memset(buf[:, 0:PH:PH - 1, :], 0.0).then_inc(zeroed, 1)
                nc.gpsimd.memset(buf[:, 1:PH - 1, 0:PW:PW - 1], 0.0).then_inc(zeroed, 1)
            nc.gpsimd.memset(stat[:], 0.0).then_inc(zeroed, 1)
            for p in range(2):
                nc.gpsimd.memset(V[p][:].rearrange("p k t w -> p (k t) w")[:, :, 0:PW:PW - 1], 0.0).then_inc(zeroed, 1)
            pool.wait_ge(zeroed, 1)
            pool.wait_ge(bn_ve_ready, 1)
            nc.gpsimd.tensor_tensor(bn_rs[:], bn_ve[:], nhalf[:, 0:1], ALU.pow).then_inc(bn_rs_ready, 1)

            def first_transform(k):
                pool.wait_ge(xn_ready, 1)
                a, b, op = transform_rows(k)
                nc.gpsimd.tensor_tensor(V[0][:, k, :, 1:1 + W], xn[:, a:a + H - 1:2, 1:1 + W],
                                        xn[:, b:b + H - 1:2, 1:1 + W], op).then_inc(v_pool_ready, 1)

            def sum_g2(i):
                pool.wait_ge(mix_first, K + i if i > 0 else 2)
                for e in range(1, E):
                    pool.wait_ge(scaled_ready, (E - 1) * i + e)
                    if e > 1:
                        pool.wait_ge(summed, (E - 1) * i + e - 1)
                    nc.gpsimd.tensor_tensor(U[i][:, G2, :], U[i][:, G2, :], scaled[:, e - 1, :], ALU.add) \
                      .then_inc(summed, 1)

            def compare_weights(w, op):
                pool.wait_ge(ws_loaded, 16)
                nc.gpsimd.tensor_scalar(w[:], ws_raw[:], 0.0, None, op).then_inc(ws_ready, 1)

            def norm_power(t):
                if chained(t):
                    pool.wait_ge(norm_ready, t + 3)
                    nc.gpsimd.tensor_tensor(rstd[:], ve, nhalf[:], ALU.pow).then_inc(rstd_ready, 1)

            def first_low_part():
                pool.wait_ge(hn_ready, 1)
                pool.wait_ge(hi_ready, 1)
                nc.gpsimd.tensor_tensor(lo[0][:, 1:1 + H, 1:1 + W], hn[:].rearrange("p (h w) -> p h w", h=H),
                                        hi[0][:, 1:1 + H, 1:1 + W], ALU.subtract).then_inc(lo_ready, 1)

            def step(t, p):
                if at(t, 1):
                    first_low_part()
                if at(t, -1):
                    first_transform(2)
                    sum_g2(0)
                    first_transform(1)
                    first_transform(3)
                if at(t, 0):
                    compare_weights(ws_pos, ALU.is_gt)
                    sum_g2(1)
                    compare_weights(ws_neg, ALU.is_lt)
                    pool.wait_ge(ws_ready, 2)
                    nc.gpsimd.tensor_tensor(ws[:], ws_pos[:], ws_neg[:], ALU.subtract).then_inc(ws_ready, 1)
                norm_power(t)

            pipeline(pool, step)

        @block.tensor
        def _(pe):
            def warm(products):
                for n in range(products):
                    nc.tensor.matmul(ps_warm[:, 0:C], ones[:], ones[:], start=True, stop=True)

            def route_logits(i):
                if has(i):
                    pe.wait_ge(pooled_ready, i + 1)
                    nc.tensor.matmul(ps_logits, ones[:], pooled[:], start=True, stop=True) \
                      .then_inc(plogits_ready, 1)

            def condconv_row(t, p, n):
                if not has(t):
                    return
                k = MORDER[n]
                if at(t, 0):
                    if n == 0:
                        pe.wait_ge(v_ready, 1)
                    else:
                        pe.wait_ge(v_pool_ready, n)
                else:
                    pe.wait_ge(v_ready, NU * t + n + 1 - (NU - 1))
                if k == 0:
                    pe.wait_ge(mixed, mixed_before(t) + E - 1)
                elif k == 2:
                    pe.wait_ge(kernel_ready, 3 * t + 2)
                elif k == 1:
                    pe.wait_ge(kernel_ready, 3 * t + 3)
                if k == 2:
                    wait(pe, m2_copied, t)
                elif k == 1:
                    wait(pe, m12_ready, 2 * t)
                else:
                    wait(pe, y_ready, 2 * t - (1 if k == 0 else 0))
                for kx in range(K):
                    mm = nc.tensor.matmul(pm[k][:], U[p][:, SLOT[k], kx * C:(kx + 1) * C],
                                          V[p][:, k, :, kx:kx + W], start=(kx == 0), stop=(kx == K - 1))
                mm.then_inc(m_ready, 1)

            def product(p, part, tap, first, last):
                ky, kx = tap // K, tap % K
                mm = nc.tensor.matmul(conv_psum(first, last), ws[:, tap * C:(tap + 1) * C],
                                      (hi, lo)[part][p][:, first // W + ky:last // W + ky, kx:kx + W],
                                      start=(part == 0 and tap == 0), stop=(part == 1 and tap == K * K - 1))
                if part == 1 and tap == K * K - 1:
                    mm.then_inc(conv_ready, 1)

            def sign_conv(i, p):
                pe.wait_ge(hi_ready, i + 1)
                wait(pe, out_ready, i)
                for part in range(2):
                    if part == 1:
                        pe.wait_ge(lo_ready, i + 1)
                    for half in range(2):
                        for tap in range(K * K):
                            product(p, part, tap, half * BANK, (half + 1) * BANK)

            def sign_conv_last(p):
                one, two, three = out_parts(B - 1)
                for part, (first, last) in ((0, two), (0, one), (1, one), (1, two), (0, three), (1, three)):
                    if part == 0 and (first, last) == two:
                        pe.wait_ge(hi_ready, B)
                        pe.wait_ge(out_ready, sums_before(B - 1) - 1)
                    if part == 0 and (first, last) == one:
                        pe.wait_ge(hi_ready, B + 1)
                        pe.wait_ge(out_ready, sums_before(B - 1))
                    if part == 1 and (first, last) == one:
                        pe.wait_ge(lo_ready, B)
                    if part == 0 and (first, last) == three:
                        pe.wait_ge(y_ready, 2 * B)
                    for tap in range(K * K):
                        product(p, part, tap, first, last)

            def step(t, p):
                if at(t, -2) or at(t, -1):
                    if at(t, -1):
                        warm(WARM[0])
                    route_logits(t + 1)
                    if at(t, -1):
                        warm(WARM[1])
                    return
                for n in range(NU):
                    condconv_row(t, p, n)
                    if n == (2 if at(t, 0) else NU - 1 if at(t, 1) else 1):
                        route_logits(t + 1)
                if at(t, 1):
                    pe.wait_ge(ws_ready, 3)
                if at(t, B):
                    sign_conv_last(1 - p)
                elif has(t - 1):
                    sign_conv(t - 1, 1 - p)

            pe.wait_ge(zeroed, 2)
            pe.wait_ge(prm_loaded, 16)
            pipeline(pe, step)

        @block.scalar
        def _(act):
            def stats_in(i, p):
                if has(i):
                    apart(act)
                    act.wait_ge(x_loaded[p], 16 * (i // 2 + 1) if isinstance(i, int) else 8 * (i - p) + 16)
                    wait(act, statT_ready, i)
                    nc.scalar.activation(junk[:], img(i), ACT.Identity, scale=1.0 / HW,
                                         accum_out=mean[:, IN:IN + 1]).then_inc(mean_in_ready, 1)
                    act.wait_ge(mean_in_ready, i + 1)
                    channel_var(i, IN, nmean_in_ready, var_in_ready)

            def stats_mid(i):
                if has(i) and not at(i, B - 1):
                    act.wait_ge(mean_mid_ready, i + 1)
                    act.wait_ge(statT_ready, i + 2)
                    channel_var(i, MID, nmean_mid_ready, var_mid_ready)

            def channel_var(i, col, nmean_ready, var_ready):
                c = slice(col, col + 1)
                nc.scalar.activation(nmean[:, c], mean[:, c], ACT.Copy, scale=-HW ** -0.5).then_inc(nmean_ready, 1)
                apart(act)
                act.wait_ge(nmean_ready, i + 1)
                nc.scalar.activation(junk[:], img(i), ACT.Square, bias=nmean[:, c], scale=HW ** -0.5,
                                     accum_out=var[:, c]).then_inc(var_ready, 1)

            def normalise(i):
                if has(i):
                    apart(act)
                    act.wait_ge(gbias_ready, i + 1)
                    nc.scalar.activation(xn[:, 1:1 + H, 1:1 + W],
                                         img(i).rearrange("p (h w) -> p h w", h=H), ACT.Identity,
                                         bias=gbias[:, IN:IN + 1], scale=rstd[:, IN:IN + 1]).then_inc(xn_ready, 1)

            def routing(i, p):
                if has(i):
                    act.wait_ge(plogits_ready, i + 1)
                    nc.scalar.activation(th[:], ps_logits, ACT.Tanh, scale=0.5).then_inc(tanh_ready, 1)
                    act.wait_ge(tanh_ready, i + 1)
                    if not isinstance(i, int) or i >= 2:
                        act.wait_ge(mixed, mixed_before(i - 1))
                    nc.scalar.activation(route[p][:], th[:], ACT.Copy, bias=0.5, scale=0.5).then_inc(route_ready, 1)

            def mix(i, p):
                if not has(i):
                    return
                act.wait_ge(route_ready, i + 1)
                wait(act, m_ready, NU * (i - 1))

                def expert0(first, last):
                    nc.scalar.activation(U[p][:, first:last + 1, :].rearrange("p k n -> p (k n)"),
                                         we[:, 0, first:last + 1, :].rearrange("p k n -> p (k n)"), ACT.Copy,
                                         scale=route[p][:, 0:1]).then_inc(mix_first, 1)

                def scale_g2(e):
                    nc.scalar.activation(scaled[:, e - 1, :], we[:, e, G2, :], ACT.Copy,
                                         scale=route[p][:, e:e + 1]).then_inc(scaled_ready, 1)

                if at(i, 0):
                    act.wait_ge(we_loaded[G0], 16)
                    expert0(G0, G0)
                    act.wait_ge(we_loaded[G2], 16)
                    expert0(G2, G2)
                    scale_g2(1)
                    act.wait_ge(we_loaded[G1], 16)
                    expert0(G1, G1)
                    scale_g2(2)
                    scale_g2(3)
                else:
                    expert0(G0, G1)
                    if is_early(i):
                        act.wait_ge(summed, (E - 1) * i)
                        for e in range(1, E):
                            scale_g2(e)

            def split(i, p):
                split_hi(i, p)
                split_hn(i)

            def split_hi(i, p):
                if has(i):
                    apart(act)
                    act.wait_ge(gbias_ready, i + 3)
                    for first, last in ((0, H // 2 + 1), (H // 2 + 1, H)) if at(i, B - 1) else ((0, H),):
                        nc.scalar.activation(hi[p][:, 1 + first:1 + last, 1:1 + W],
                                             img(i).rearrange("p (h w) -> p h w", h=H)[:, first:last, :], ACT.Identity,
                                             bias=gbias[:, MID:MID + 1], scale=rstd[:, MID:MID + 1]) \
                          .then_inc(hi_ready, 1)

            def split_hn(i):
                if has(i):
                    nc.scalar.activation(hn[:], img(i), ACT.Identity, bias=gbias[:, MID:MID + 1],
                                         scale=rstd[:, MID:MID + 1]).then_inc(hn_ready, 1)

            def copy_m2(i):
                if has(i):
                    act.wait_ge(m_ready, NU * i + 2)
                    wait(act, m12_ready, 2 * i)
                    nc.scalar.activation(m2s[:], pm[2][:], ACT.Copy, scale=0.5).then_inc(m2_copied, 1)

            def silu(i):
                if at(i, B - 1):
                    for odd in range(2):
                        act.wait_ge(y_ready, 2 * i + 1 + odd)
                        nc.scalar.activation(y[:, odd:H:2, :], y[:, odd:H:2, :], ACT.Silu, bias=bn_shift[:, 0:1],
                                             scale=bn_scale[:, 0:1]).then_inc(silu_ready, 1)
                elif has(i):
                    act.wait_ge(y_ready, 2 * i + 2)
                    nc.scalar.activation(y[:], y[:], ACT.Silu, bias=bn_shift[:, 0:1],
                                         scale=bn_scale[:, 0:1]).then_inc(silu_ready, 1)

            def step(t, p):
                if at(t, 1):
                    copy_m2(t)
                    split_hi(t - 1, 1 - p)
                    normalise(t + 1)
                    split_hn(t - 1)
                else:
                    normalise(t + 1)
                if at(t, 0):
                    copy_m2(t)
                routing(t + 1, 1 - p)
                mix(t + 1, 1 - p)
                if at(t, B - 1):
                    split(t - 1, 1 - p)
                    copy_m2(t)
                elif not at(t, 0) and not at(t, 1):
                    copy_m2(t)
                    split(t - 1, 1 - p)
                if at(t, 1):
                    silu(t)
                if not at(t, -2):
                    stats_in(t + 2, p)
                if at(t, 0):
                    act.wait_ge(bn_ready, 4)
                if not at(t, 1):
                    silu(t)
                stats_mid(t)

            act.wait_ge(zeroed, 1)
            nc.scalar.activation(warm_out[:], nhalf[:, 0:1], ACT.Silu)
            act.wait_ge(zeroed, 15)
            pipeline(act, step)

        @block.vector
        def _(dve):
            v = nc.vector

            def chain_start(t):
                if not chained(t):
                    return
                n = t + 3
                groups = lambda ap: ap.rearrange("p (g k) -> p g k", k=GSIZE)
                spread_out = lambda ap: ap[:].unsqueeze(2).to_broadcast([C, SG, GSIZE])
                devT = normT[:, 2 * SQ:3 * SQ]
                if has(t + 2):
                    dve.wait_ge(var_in_ready, t + 3)
                if has(t):
                    dve.wait_ge(mean_mid_ready, t + 1)
                    dve.wait_ge(var_mid_ready, t + 1)
                v.transpose(statT[:], stat[:]).then_inc(statT_ready, 1)
                dve.wait_ge(statT_ready, n)
                v.tensor_reduce(gsumT[:], groups(statT[:, 0:SQ]), AX_X, ALU.add).then_inc(gsumT_ready, 1)
                dve.wait_ge(gsumT_ready, n)
                v.scalar_tensor_tensor(out=groups(devT), in0=spread_out(gsumT), scalar=-1.0 / GSIZE,
                                       in1=groups(statT[:, 0:SQ]), op0=ALU.mult, op1=ALU.add) \
                 .then_inc(normT_ready, 1)
                v.tensor_scalar(groups(normT[:, SQ:2 * SQ]), spread_out(gsumT), -1.0 / GSIZE, None, ALU.mult) \
                 .then_inc(normT_ready, 1)
                dve.wait_ge(normT_ready, 3 * n - 2)
                v.tensor_tensor(dev2T[:], devT, devT, ALU.mult).then_inc(dev2T_ready, 1)
                dve.wait_ge(dev2T_ready, n)
                v.tensor_tensor(spreadT[:], dev2T[:], statT[:, SQ:2 * SQ], ALU.add).then_inc(spreadT_ready, 1)
                dve.wait_ge(spreadT_ready, n)
                v.tensor_reduce(gspreadT[:], groups(spreadT[:]), AX_X, ALU.add).then_inc(gspreadT_ready, 1)
                dve.wait_ge(gspreadT_ready, n)
                v.tensor_scalar(groups(normT[:, 0:SQ]), spread_out(gspreadT), 1.0 / (GSIZE * ACT_SCALE ** 2),
                                GN_EPS / ACT_SCALE ** 2, ALU.mult, ALU.add).then_inc(normT_ready, 1)
                dve.wait_ge(normT_ready, 3 * n)
                v.transpose(norm[:], normT[:]).then_inc(norm_ready, 1)

            def chain_end(t):
                if not chained(t):
                    return
                dve.wait_ge(rstd_ready, t + 3)
                v.tensor_tensor(gbias[:], ngmean, rstd[:], ALU.mult).then_inc(gbias_ready, 1)
                if has(t + 2):
                    v.tensor_scalar(contrib[:], wroute[:], dev_in, rstd[:, IN:IN + 1], ALU.mult, ALU.mult) \
                     .then_inc(contrib_ready, 1)
                    dve.wait_ge(contrib_ready, t + 3)
                    v.tensor_tensor(pooled[:], contrib[:], bshare[:], ALU.add).then_inc(pooled_ready, 1)

            def transform(i, p, k):
                if not has(i):
                    return
                if k == MORDER[0]:
                    dve.wait_ge(xn_ready, i + 1)
                    wait(dve, m_ready, NU * (i - 1))
                a, b, op = transform_rows(k)
                v.tensor_tensor(V[p][:, k, :, 1:1 + W], xn[:, a:a + H - 1:2, 1:1 + W],
                                xn[:, b:b + H - 1:2, 1:1 + W], op).then_inc(v_ready, 1)

            def mix_row(i, g):
                n = mixed_before(i) + (E - 1) * (g == G1)
                dve.wait_ge(mix_first, 1 if i == 0 and g == G0 else i + K)
                dve.wait_ge(we_loaded[g], 16)
                for e in range(1, E):
                    if e > 1:
                        dve.wait_ge(mixed, n + e - 1)
                    v.scalar_tensor_tensor(out=U[i][:, g, :], in0=we[:, e, g, :], scalar=route[i][:, e:e + 1],
                                           in1=U[i][:, g, :], op0=ALU.mult, op1=ALU.add).then_inc(mixed, 1)

            def mix(i, p, e):
                if has(i):
                    if e == 1:
                        dve.wait_ge(mix_first, i + K)
                    else:
                        dve.wait_ge(mixed, mixed_before(i) + e - 1)
                    u = U[p][:, 0:K, :].rearrange("p k n -> p (k n)")
                    v.scalar_tensor_tensor(out=u, in0=we[:, e, :, :].rearrange("p k n -> p (k n)"),
                                           scalar=route[p][:, e:e + 1], in1=u, op0=ALU.mult, op1=ALU.add) \
                     .then_inc(mixed, 1)

            def kernel_rows(i, p):
                if has(i):
                    dve.wait_ge(mixed, mixed_before(i + 1))
                    if is_early(i):
                        dve.wait_ge(summed, (E - 1) * (i + 1))
                    v.tensor_tensor(g02[:], U[p][:, G0, :], U[p][:, G2, :], ALU.add).then_inc(kernel_ready, 1)
                    dve.wait_ge(kernel_ready, 3 * i + 1)
                    v.tensor_tensor(U[p][:, SLOT[2], :], g02[:], U[p][:, G1, :], ALU.subtract).then_inc(kernel_ready, 1)
                    v.tensor_tensor(U[p][:, SLOT[1], :], g02[:], U[p][:, G1, :], ALU.add).then_inc(kernel_ready, 1)

            def low_part(i, p):
                if has(i):
                    dve.wait_ge(hn_ready, i + 1)
                    dve.wait_ge(hi_ready, B + 1 if at(i, B - 1) else i + 1)
                    v.tensor_tensor(lo[p][:, 1:1 + H, 1:1 + W], hn[:].rearrange("p (h w) -> p h w", h=H),
                                    hi[p][:, 1:1 + H, 1:1 + W], ALU.subtract).then_inc(lo_ready, 1)

            def inverse(i, part):
                if not has(i):
                    return
                rows = y[:].rearrange("p (t two) w -> p two t w", two=2)
                view = lambda ap: ap.rearrange("p (t w) -> p t w", t=TILES)
                if part == 0:
                    dve.wait_ge(m2_copied, i + 1)
                    dve.wait_ge(m_ready, NU * i + 3)
                    wait(dve, y_ready, 2 * i)
                    for half, op in ((0, ALU.add), (1, ALU.subtract)):
                        v.scalar_tensor_tensor(out=m12[:, half, :], in0=pm[1][:], scalar=0.5, in1=m2s[:],
                                               op0=ALU.mult, op1=op).then_inc(m12_ready, 1)
                elif part == 1:
                    dve.wait_ge(m12_ready, 2 * i + 1)
                    v.tensor_tensor(rows[:, 0, :, :], view(m12[:, 0, :]), view(pm[0][:]), ALU.add).then_inc(y_ready, 1)
                else:
                    dve.wait_ge(m12_ready, 2 * i + 2)
                    dve.wait_ge(m_ready, NU * i + 4)
                    v.tensor_tensor(rows[:, 1, :, :], view(m12[:, 1, :]), view(pm[3][:]), ALU.subtract) \
                     .then_inc(y_ready, 1)

            def half_stats(i, half, ready):
                v.bn_stats(halves[:, half, :], img(i)[:, half * BANK:(half + 1) * BANK]).then_inc(ready, 1)

            def residual_last():
                dve.wait_ge(silu_ready, B + 1)
                for half in range(2):
                    part = img(B - 1)[:, half * BANK:(half + 1) * BANK]
                    rows = y[:, half * (H // 2):(half + 1) * (H // 2), :].rearrange("p h w -> p (h w)")
                    v.tensor_tensor(part, rows, part, ALU.add).then_inc(h_ready, 1)
                for half, ready in ((0, mean_mid_ready), (1, nmean_mid_ready)):
                    dve.wait_ge(h_ready, B + half)
                    half_stats(B - 1, half, ready)
                dve.wait_ge(mean_mid_ready, B)
                dve.wait_ge(nmean_mid_ready, B)
                v.bn_aggr(stat[:, MID:MID + SQ + 1:SQ], halves[:]).then_inc(var_mid_ready, 1)

            def residual(i):
                if at(i, B - 1):
                    residual_last()
                elif has(i):
                    dve.wait_ge(silu_ready, i + 1)
                    v.scalar_tensor_tensor(out=img(i), in0=y[:].rearrange("p h w -> p (h w)"), scalar=1.0, in1=img(i),
                                           op0=ALU.mult, op1=ALU.add, accum_out=hsum[:]).then_inc(h_ready, 1)
                    dve.wait_ge(h_ready, i + 1)
                    v.tensor_scalar(mean[:, MID:MID + 1], hsum[:], 1.0 / HW, None, ALU.mult).then_inc(mean_mid_ready, 1)

            def output(i):
                if has(i):
                    dve.wait_ge(conv_ready, 2 * i + 2)
                    v.scalar_tensor_tensor(out=img(i), in0=pc[:].rearrange("p a n -> p (a n)"),
                                           scalar=1.0 / ACT_SCALE, in1=img(i), op0=ALU.mult, op1=ALU.add) \
                     .then_inc(out_ready, 1)

            def output_part(i, n):
                first, last = out_parts(i)[n]
                dve.wait_ge(conv_ready, 2 * i + 1 + n)
                part = img(i)[:, first:last]
                v.scalar_tensor_tensor(out=part, in0=conv_psum(first, last), scalar=1.0 / ACT_SCALE, in1=part,
                                       op0=ALU.mult, op1=ALU.add) \
                 .then_inc(out_ready, 1)

            def step(t, p):
                if at(t, -2):
                    chain_start(t)
                    batch_norm_parameters()
                elif at(t, -1):
                    first_kernels()
                elif at(t, 0):
                    first_image()
                elif at(t, 1):
                    second_image()
                elif at(t, B):
                    output_part(B - 2, 0)
                    chain_end(B - 1)
                    output_part(B - 2, 1)
                    low_part(B - 1, 1 - p)
                elif at(t, B + 1):
                    for n in range(len(out_parts(B - 1))):
                        output_part(B - 1, n)
                else:
                    output(t - 2)
                    chain_end(t - 1)
                    for k in MORDER:
                        transform(t + 1, 1 - p, k)
                    mix(t + 1, 1 - p, 1)
                    mix(t + 1, 1 - p, 2)
                    if at(t, B - 1):
                        low_part(t - 1, 1 - p)
                    for part in range(3):
                        inverse(t, part)
                    if not at(t, B - 1):
                        low_part(t - 1, 1 - p)
                    residual(t)
                    mix(t + 1, 1 - p, 3)
                    kernel_rows(t + 1, 1 - p)
                    chain_start(t)

            def first_kernels():
                chain_end(-2)
                transform(0, 0, 0)
                mix_row(0, G0)
                mix_row(0, G1)
                kernel_rows(0, 0)
                chain_start(-1)
                dve.wait_ge(v_pool_ready, 3)
                chain_end(-1)

            def first_image():
                transform(1, 1, 0)
                transform(1, 1, 2)
                inverse(0, 0)
                inverse(0, 1)
                mix_row(1, G0)
                inverse(0, 2)
                mix_row(1, G1)
                kernel_rows(1, 1)
                residual(0)
                transform(1, 1, 1)
                transform(1, 1, 3)
                chain_start(0)

            def second_image():
                inverse(1, 0)
                chain_end(0)
                inverse(1, 1)
                inverse(1, 2)
                for k in MORDER:
                    transform(2, 0, k)
                mix(2, 0, 1)
                mix(2, 0, 2)
                residual(1)
                mix(2, 0, 3)
                kernel_rows(2, 0)
                chain_start(1)
                dve.wait_ge(lo_ready, 1)

            def batch_norm_parameters():
                dve.wait_ge(bn_rs_ready, 1)
                v.tensor_tensor(bn_scale[:], bn_rs[:], prm[:, P_GAMMA:P_GAMMA + 1], ALU.mult).then_inc(bn_ready, 1)
                dve.wait_ge(bn_ready, 1)
                v.tensor_tensor(bn_mscale[:], bn_scale[:], prm[:, P_MEAN:P_MEAN + 1], ALU.mult).then_inc(bn_ready, 1)
                dve.wait_ge(bn_ready, 2)
                v.tensor_tensor(bn_shift[:], prm[:, P_BETA:P_BETA + 1], bn_mscale[:], ALU.subtract) \
                 .then_inc(bn_ready, 1)
                v.tensor_scalar(bn_scale[:], bn_scale[:], 1.0 / ACT_SCALE, None, ALU.mult).then_inc(bn_ready, 1)

            dve.wait_ge(zeroed, 15)
            dve.wait_ge(x_half_loaded, 16)
            half_stats(0, 0, mean_in_ready)
            dve.wait_ge(x_loaded[0], 16)
            half_stats(0, 1, nmean_in_ready)
            dve.wait_ge(mean_in_ready, 1)
            dve.wait_ge(nmean_in_ready, 1)
            v.bn_aggr(stat[:, IN:IN + SQ + 1:SQ], halves[:]).then_inc(var_in_ready, 1)
            dve.wait_ge(prm_loaded, 16)
            v.tensor_scalar(bn_ve[:], prm[:, P_VAR:P_VAR + 1], BN_EPS, None, ALU.add).then_inc(bn_ve_ready, 1)
            v.tensor_scalar(bshare[:], prm[:, P_BROUTE:P_BROUTE + E], 1.0 / C, None, ALU.mult) \
             .then_inc(route_prm_ready, 1)
            v.tensor_scalar(wroute[:], prm[:, P_WROUTE:P_WROUTE + E], 1.0 / ACT_SCALE, None, ALU.mult) \
             .then_inc(route_prm_ready, 1)
            dve.wait_ge(route_prm_ready, 2)
            pipeline(dve, step)


def kernel(x, L0_conv_w_route, L0_conv_b_route, L0_conv_w_experts, L0_conv_bn_gamma, L0_conv_bn_beta,
           L0_conv_bn_mean, L0_conv_bn_var, L1_conv_W):
    import concourse.bacc as bacc
    from concourse.bass_utils import run_bass_kernel_spmd

    lay = np.ascontiguousarray
    bn = [np.asarray(a)[:, None] for a in (L0_conv_bn_gamma, L0_conv_bn_beta, L0_conv_bn_mean, L0_conv_bn_var)]
    params = bn + [np.asarray(L0_conv_w_route).T, np.broadcast_to(np.asarray(L0_conv_b_route)[None, :], (C, E))]
    arrays = {
        "x": lay(x),
        "w_experts": lay(np.transpose(np.asarray(L0_conv_w_experts), (2, 3, 0, 4, 1))),
        "w_sign": lay(np.transpose(np.asarray(L1_conv_W), (1, 2, 3, 0))),
        "params": lay(np.concatenate(params, axis=1)),
    }
    nc = bacc.Bacc("TRN2", target_bir_lowering=False, num_devices=1)
    args = [nc.dram_tensor(n, a.shape, mybir.dt.from_np(a.dtype), kind="ExternalInput").ap() for n, a in arrays.items()]
    out = nc.dram_tensor("out", (B, C, H, W), F32, kind="ExternalOutput").ap()
    build(nc, *args, out)
    r = run_bass_kernel_spmd(nc, [arrays], core_ids=[0])
    return r.results[0]["out"]
```
